# Optimizing a Trainium2 kernel written in Bass

```python
import numpy as np
import jax
import jax.numpy as jnp

def _softmax(x, axis=-1):
    return jax.nn.softmax(x, axis=axis)

def _gelu(x):
    return jax.nn.gelu(x, approximate=True)

def _silu(x):
    return jax.nn.silu(x)

def _sigmoid(x):
    return jax.nn.sigmoid(x)

def _layernorm(x, axis=-1, eps=1e-05):
    m = jnp.mean(x, axis=axis, keepdims=True)
    v = jnp.var(x, axis=axis, keepdims=True)
    return (x - m) / jnp.sqrt(v + eps)

def _scatter_add(tgt, idx, src, axis=0):
    return tgt.at[idx].add(src)

def _segment_sum(src, seg, n):
    return jax.ops.segment_sum(src, seg, n)
kernel_name = 'mk_rec_standalone_d1_rec_r8_331644'

def setup_inputs(seed: int=0):
    np.random.seed(seed)
    _w = jnp.asarray

    def _rec_inputs():
        import jax
        import jax.numpy as jnp
        _rk = jax.random.key(seed)
        r_transformer_out = -0.000161372 + 0.999968 * jax.random.normal(jax.random.fold_in(_rk, 1), (512, 200, 128), jnp.float32)
        r_candidate = 0.00222621 + 0.99962 * jax.random.normal(jax.random.fold_in(_rk, 2), (512, 128), jnp.float32)
        r_mask = jax.random.bernoulli(jax.random.fold_in(_rk, 3), 0.5005, (512, 200))
        return (r_transformer_out, r_candidate, r_mask)
    r_transformer_out, r_candidate, r_mask = _rec_inputs()

    def _L0_rec_setup():
        import jax, jax.numpy as jnp
        import numpy as np
        D = 128
        H = 128
        key = jax.random.key(seed)
        ks = jax.random.split(key, 8)
        B, T = (512, 200)
        transformer_out = jax.random.normal(ks[0], (B, T, D), dtype=jnp.float32)
        candidate = jax.random.normal(ks[1], (B, D), dtype=jnp.float32)
        mask = jax.random.randint(ks[2], (B, T), 0, 2).astype(jnp.bool_)
        lim1 = 1.0 / np.sqrt(3 * D)
        W1 = jax.random.uniform(ks[3], (3 * D, H), minval=-lim1, maxval=lim1, dtype=jnp.float32)
        b1 = jax.random.uniform(ks[4], (H,), minval=-lim1, maxval=lim1, dtype=jnp.float32)
        a = jnp.array(0.25, dtype=jnp.float32)
        lim2 = 1.0 / np.sqrt(H)
        W2 = jax.random.uniform(ks[5], (H, 1), minval=-lim2, maxval=lim2, dtype=jnp.float32)
        b2 = jax.random.uniform(ks[6], (1,), minval=-lim2, maxval=lim2, dtype=jnp.float32)
        return {'transformer_out': transformer_out, 'candidate': candidate, 'mask': mask, 'W1': W1, 'b1': b1, 'a': a, 'W2': W2, 'b2': b2}
    _L0_rec_all = _L0_rec_setup()
    _L0_rec_in = {k: v for k, v in _L0_rec_all.items() if k in ('W1', 'b1', 'a', 'W2', 'b2')}
    del _L0_rec_all
    return {'r_transformer_out': r_transformer_out, 'r_candidate': r_candidate, 'r_mask': r_mask, 'L0_rec_W1': _L0_rec_in['W1'], 'L0_rec_b1': _L0_rec_in['b1'], 'L0_rec_a': _L0_rec_in['a'], 'L0_rec_W2': _L0_rec_in['W2'], 'L0_rec_b2': _L0_rec_in['b2']}

def reference(r_transformer_out, r_candidate, r_mask, L0_rec_W1, L0_rec_b1, L0_rec_a, L0_rec_W2, L0_rec_b2):
    import jax
    import jax.numpy as jnp

    def _L0_rec_ref(transformer_out, candidate, mask, W1, b1, a, W2, b2):
        import jax, jax.numpy as jnp
        import numpy as np
        D = 128
        H = 128
        cand_exp = jnp.broadcast_to(candidate[:, None, :], transformer_out.shape)
        att_input = jnp.concatenate([transformer_out, cand_exp, transformer_out * cand_exp], axis=-1)
        h = att_input @ W1 + b1
        h = jnp.where(h >= 0, h, a * h)
        scores = (h @ W2 + b2)[..., 0]
        scores = jnp.where(mask, scores, -jnp.inf)
        weights = jax.nn.softmax(scores, axis=-1)
        return jnp.einsum('bt,btd->bd', weights, transformer_out)
    y = _L0_rec_ref(r_transformer_out, r_candidate, r_mask, L0_rec_W1, L0_rec_b1, L0_rec_a, L0_rec_W2, L0_rec_b2)
    return y

_drawn_inputs = setup_inputs


def setup_inputs(seed=0):
    import zlib

    import numpy as np

    out = dict(_drawn_inputs(seed))
    spreads = {}
    factors = {'L0_rec_b1': 8.0}
    for name, (base, spread) in spreads.items():
        noise = np.random.default_rng([zlib.crc32(name.encode()), seed]).standard_normal(out[name].shape)
        drawn = base * np.exp(spread * noise) if base else spread * noise
        out[name] = jnp.asarray(drawn.astype(out[name].dtype))
    for name, factor in factors.items():
        out[name] = (out[name] * factor).astype(out[name].dtype)
    return out
```

```python
from contextlib import ExitStack

import concourse.bass as bass
from concourse import mybir

ROWS, TOKENS, D, H = 512, 200, 128, 128
P = 128
GROUP = 16
GROUPS = ROWS // GROUP
Q = P // GROUP
J = TOKENS // Q
QUADS = 4
RUNS = GROUP // QUADS
PAIRS = GROUP // 2
HALF = GROUP // 2

X_SLOTS = 4
X_CUT = 12
H_BANKS = 4
T_BANKS = 2
T_BATCH = 4
CHUNKS = [list(range(j, min(j + T_BATCH, J))) for j in range(0, J, T_BATCH)]
ACT_CHUNKS = [0, 2, 3, 5]
DVE_CHUNKS = [1, 4, 6]
POOL_ROWS = 10
LAPS = (2, 30)
MASKED = -3e38
LEAST_MAX = -1e38


def row_of(n):
    return RUNS * (n % QUADS) + n // QUADS


class Step:

    def __init__(self, lap, c):
        self.lap, self.c = lap, c

    def at(self, mult, add=0):
        return self.lap * (X_SLOTS * mult) + (self.c * mult + add)

    def lap_of(self, d, mult, add=0):
        return self.lap * mult + ((self.c + d) // X_SLOTS * mult + add)

    def pairs_of(self, d, mult, add=0):
        return self.lap * (X_SLOTS // 2 * mult) + ((self.c + d) // 2 * mult + add)

    def slot(self, d, n=X_SLOTS):
        return (self.c + d) % n

    def has(self, d):
        return not isinstance(self.lap, int) or 0 <= self.c + d < GROUPS


def run_steps(engine, step):
    for c in range(0, LAPS[0]):
        step(Step(0, c))
    with engine.Fori(0, (LAPS[1] - LAPS[0]) // X_SLOTS) as lap:
        for c in range(LAPS[0], LAPS[0] + X_SLOTS):
            step(Step(lap, c))
    for c in range(LAPS[1], GROUPS + 2):
        step(Step(0, c))


def build(nc, x_in, cand_in, mask_in, w1_in, b1_in, a_in, w2_in, b2_in, out):
    f32, bf16, u8, u16 = mybir.dt.float32, mybir.dt.bfloat16, mybir.dt.uint8, mybir.dt.uint16
    ALU, ACT, AX = mybir.AluOpType, mybir.ActivationFunctionType, mybir.AxisListType

    x_groups = x_in.rearrange("b t d -> (b t) d").rearrange("(k p j) d -> k p (j d)", p=P, j=J)
    out_groups = out.rearrange("(k b) d -> k b d", b=GROUP)
    mask_quads = mask_in.rearrange("(k g r) t -> g r k t", g=QUADS, r=RUNS)

    with ExitStack() as ctx:
        def sb(name, shape, dt=f32):
            return ctx.enter_context(nc.sbuf_tensor(name, shape, dt))

        def sem(name):
            return ctx.enter_context(nc.semaphore(name))

        x = sb("x", [P, X_SLOTS, J * D])
        xT = sb("xT", [P, 2, J, P])
        w_eff = sb("w_eff", [P, 2, GROUP, H])
        relu_neg = sb("relu_neg", [P, H_BANKS, 2, TOKENS])
        act_out = sb("act_out", [P, GROUP, TOKENS])
        cand_bias = sb("cand_bias", [P, GROUPS, 2, GROUP])
        stage = sb("stage", [P, X_SLOTS, 2, GROUP])
        mask_b = sb("mask_b", [P, GROUPS * TOKENS], u8)
        mask_add = sb("mask_add", [P, GROUPS * TOKENS], bf16)
        score = sb("score", [P, Q, J])
        prob = sb("prob", [P, TOKENS])
        weight = sb("weight", [P, TOKENS])
        w_col = sb("w_col", [P, J])
        w_diag = sb("w_diag", [P, 2, J, GROUP])
        part = sb("part", [P, D])
        y = sb("y", [GROUP, 2, D])
        cand = sb("cand", [P, ROWS // P, D])
        w1 = sb("w1", [P, 3, H])
        w2_slide = sb("w2_slide", [P, 2 * RUNS - 1])
        ident = sb("ident", [P, P])
        row_mask = sb("row_mask", [P, GROUP])
        quad_sum = sb("quad_sum", [P, GROUP])
        b1 = sb("b1", [P, 1])
        a = sb("a", [P, 1])
        one_less_a = sb("one_less_a", [P, 1])
        b2 = sb("b2", [P, 1])
        row_const = sb("row_const", [P, GROUPS])
        neg_top = sb("neg_top", [P, 1])
        neg_max = sb("neg_max", [P, 1])
        total = sb("total", [P, 1])
        inv_total = sb("inv_total", [P, 1])

        t_bank = [ctx.enter_context(nc.psum_tensor(f"t_bank{i}", [P, 512], f32)) for i in range(T_BANKS)]
        h_bank = [ctx.enter_context(nc.psum_tensor(f"h_bank{i}", [P, 512], f32)) for i in range(H_BANKS)]
        s_bank = ctx.enter_context(nc.psum_tensor("s_bank", [P, 512], f32))
        o_bank = ctx.enter_context(nc.psum_tensor("o_bank", [P, 512], f32))
        part_ps, y_ps = o_bank[:, 0:D], o_bank[0:GROUP, D:2 * D]

        x_loaded = [[sem(f"x_loaded{s}_{h}") for h in range(2)] for s in range(X_SLOTS)]
        cand_loaded, w1_loaded, small_loaded, mask_loaded = (
            sem("cand_loaded"), sem("w1_loaded"), sem("small_loaded"), sem("mask_loaded"))
        zeros_set, ident_set, masks_set = sem("zeros_set"), sem("ident_set"), sem("masks_set")
        mask_cleared, mask_added = sem("mask_cleared"), sem("mask_added")
        cand_turned, cand_copied = sem("cand_turned"), sem("cand_copied")
        bias_ready, bias_copied = sem("bias_ready"), sem("bias_copied")
        const_ready, const_copied, scalars_set = sem("const_ready"), sem("const_copied"), sem("scalars_set")
        staged = sem("staged")
        pool_mult = sem("pool_mult")
        pool_w, dve_w = sem("pool_w"), sem("dve_w")
        turned = sem("turned")
        act_copied, dve_copied = sem("act_copied"), sem("dve_copied")
        h_ready = sem("h_ready")
        relu_ready = sem("relu_ready")
        act_ready = sem("act_ready")
        scores_ready = sem("scores_ready")
        scores_read = sem("scores_read")
        top_ready = sem("top_ready")
        max_ready, prob_ready, inv_ready, weight_ready = (
            sem("max_ready"), sem("prob_ready"), sem("inv_ready"), sem("weight_ready"))
        w_col_loaded, w_diag_ready = sem("w_col_loaded"), sem("w_diag_ready")
        sum_ready = sem("sum_ready")
        part_copied, y_ready, y_copied = sem("part_copied"), sem("y_ready"), sem("y_copied")
        stored = [sem("stored0"), sem("stored1")]

        def chunk_copied(L_at, c):
            if c in ACT_CHUNKS:
                return act_copied, L_at(len(ACT_CHUNKS), ACT_CHUNKS.index(c) + 1)
            return dve_copied, L_at(len(DVE_CHUNKS), DVE_CHUNKS.index(c) + 1)

        def t_slot(s, c):
            return t_bank[(s.slot(1, 2) + c) % T_BANKS]

        def copy_chunk(copy, s, c):
            j, n = CHUNKS[c][0], len(CHUNKS[c])
            return copy(xT[:, s.slot(1, 2), j:j + n, :],
                        t_slot(s, c)[:, 0:n * P].rearrange("d (j p) -> d j p", p=P))

        block = ctx.enter_context(nc.Block())

        @block.sync
        def _(sp):
            def load_x(s, d):
                slot = s.slot(d)
                src = x_groups[bass.ds(s.at(1, d), 1)].rearrange("k p n -> (k p) n")
                for h, (lo, hi) in enumerate(((0, X_CUT * D), (X_CUT * D, J * D))):
                    sp.dma_start(x[:, slot, lo:hi], src[:, lo:hi]).then_inc(x_loaded[slot][h], 16)

            sp.dma_start(cand[:, :, :], cand_in.rearrange("(c p) d -> p c d", p=P)).then_inc(cand_loaded, 16)
            sp.dma_start(w1[:, :, :], w1_in.rearrange("(s d) h -> d s h", d=D)).then_inc(w1_loaded, 16)
            load_x(Step(0, 0), 0)
            sp.dma_start(b1[:, :], b1_in.rearrange("(h o) -> h o", o=1)).then_inc(small_loaded, 16)
            sp.wait_ge(zeros_set, 1)
            sp.dma_start(w2_slide[:, RUNS - 1:RUNS], w2_in).then_inc(small_loaded, 16)
            sp.dma_start(a[:, :], a_in.partition_broadcast(P)).then_inc(small_loaded, 16)
            sp.dma_start(b2[:, :], b2_in.partition_broadcast(P)).then_inc(small_loaded, 16)
            load_x(Step(0, 0), 1)
            sp.wait_ge(mask_cleared, 1)
            for g in range(QUADS):
                sp.dma_start(mask_b[32 * g:32 * g + RUNS, :].rearrange("r (k t) -> r k t", t=TOKENS),
                             mask_quads[g]).then_inc(mask_loaded, 16)

            def step(s):
                if s.has(2):
                    if s.has(-2):
                        sp.wait_ge(sum_ready, s.at(1, -1))
                    load_x(s, 2)
                if s.has(-1):
                    sp.wait_ge(weight_ready, s.at(1))
                    for g in range(QUADS):
                        sp.dma_start(w_col[32 * g:32 * g + 32, :],
                                     weight[32 * g:32 * g + RUNS, :]).then_inc(w_col_loaded, 16)
                if s.has(-2):
                    sp.wait_ge(y_copied, s.at(1, -1))
                    sp.dma_start(out_groups[bass.ds(s.at(1, -2), 1)].rearrange("k b d -> (k b) d"),
                                 y[:, s.slot(-2, 2), :]).then_inc(stored[s.slot(-2, 2)], 16)

            run_steps(sp, step)
            for half in stored:
                sp.wait_ge(half, 16 * (GROUPS // 2))

        @block.gpsimd
        def _(pool):
            nc.gpsimd.memset(ident[:, :], 0.0).then_inc(ident_set, 1)
            pool.wait_ge(ident_set, 1)
            nc.gpsimd.affine_select(out=ident[:, :], in_=ident[:, :], compare_op=ALU.not_equal, fill=1.0,
                                    base=0, pattern=[[-1, P]], channel_multiplier=1).then_inc(ident_set, 1)

            def step(s):
                if not s.has(1):
                    return
                if s.c >= 0:
                    if s.has(-1):
                        pool.wait_ge(h_ready, s.at(PAIRS))
                src = cand_bias[:, bass.ds(s.at(1, 1), 1)].rearrange("p k s n -> p (k s n)")
                nc.gpsimd.tensor_copy(stage[:, s.slot(1)].rearrange("p s n -> p (s n)"),
                                      src).then_inc(staged, 1)
                pool.wait_ge(staged, s.at(1, 2))
                rows = w_eff[:, s.slot(1, 2), 0:POOL_ROWS, :]
                nc.gpsimd.tensor_tensor(
                    rows, w1[:, 2:3, :].to_broadcast([P, POOL_ROWS, H]),
                    stage[:, s.slot(1), 0, 0:POOL_ROWS].unsqueeze(2).to_broadcast([P, POOL_ROWS, H]),
                    ALU.mult).then_inc(pool_mult, 1)
                pool.wait_ge(pool_mult, s.at(1, 2))
                nc.gpsimd.tensor_tensor(rows, rows, w1[:, 0:1, :].to_broadcast([P, POOL_ROWS, H]),
                                        ALU.add).then_inc(pool_w, 1)

            pool.wait_ge(w1_loaded, 16)
            pool.wait_ge(bias_copied, 1)
            step(Step(0, -1))
            run_steps(pool, step)

        @block.scalar
        def _(act):
            def copy_x(s, c):
                act.wait_ge(turned, s.at(len(CHUNKS), len(CHUNKS) + c + 1))
                if c == ACT_CHUNKS[0] and s.has(-1):
                    act.wait_ge(h_ready, s.at(PAIRS))
                copy_chunk(nc.scalar.copy, s, c).then_inc(act_copied, 1)

            def step(s):
                for m in range(PAIRS):
                    if s.has(0):
                        if m == 0:
                            act.wait_ge(staged, s.at(1, 1))
                        act.wait_ge(h_ready, s.at(PAIRS, m + 1))
                        for n in (2 * m, 2 * m + 1):
                            relu = nc.scalar.activation(
                                relu_neg[:, m % H_BANKS, n % 2, :],
                                h_bank[m % H_BANKS][:, (n % 2) * TOKENS:(n % 2 + 1) * TOKENS], ACT.Relu,
                                scale=-1.0, bias=stage[:, s.slot(0), 1, n:n + 1])
                        relu.then_inc(relu_ready, 1)
                        if s.has(1) and m - 1 in ACT_CHUNKS:
                            copy_x(s, m - 1)
                    if m == PAIRS // 2 - 1 and s.has(-1):
                        act.wait_ge(max_ready, s.at(1))
                        nc.scalar.activation(prob[:, :], score[:, :, :].rearrange("p q j -> p (q j)"),
                                             ACT.Exp, bias=neg_max[:, :], accum_out=total[:, :]
                                             ).then_inc(prob_ready, 1)
                    if m == PAIRS // 2 - 1 and s.has(-2):
                        act.wait_ge(sum_ready, s.at(1, -1))
                        nc.scalar.copy(part[:, :], part_ps).then_inc(part_copied, 1)
                if s.has(-2):
                    act.wait_ge(y_ready, s.at(1, -1))
                    if s.has(-4):
                        act.wait_ge(stored[s.slot(-2, 2)], s.pairs_of(-4, 16, 16))
                    nc.scalar.copy(y[:, s.slot(-2, 2), :], y_ps).then_inc(y_copied, 1)

            for c in ACT_CHUNKS:
                copy_x(Step(0, -1), c)
            act.wait_ge(mask_loaded, 16 * QUADS)
            nc.scalar.activation(mask_add[:, :], mask_b[:, :], ACT.Copy,
                                 scale=-MASKED, bias=MASKED).then_inc(mask_added, 1)
            run_steps(act, step)

        @block.vector
        def _(dve):
            def copy_x(s, c):
                dve.wait_ge(turned, s.at(len(CHUNKS), len(CHUNKS) + c + 1))
                if c == DVE_CHUNKS[0] and s.has(-1):
                    dve.wait_ge(h_ready, s.at(PAIRS))
                copy_chunk(nc.vector.tensor_copy, s, c).then_inc(dve_copied, 1)

            def build_w(s, n):
                if n == POOL_ROWS:
                    dve.wait_ge(staged, s.at(1, 2))
                    if s.has(-1):
                        dve.wait_ge(h_ready, s.at(PAIRS))
                made = nc.vector.scalar_tensor_tensor(
                    w_eff[:, s.slot(1, 2), n, :], w1[:, 2, :], stage[:, s.slot(1), 0, n:n + 1],
                    w1[:, 0, :], ALU.mult, ALU.add)
                if n == GROUP - 1:
                    made.then_inc(dve_w, 1)

            def mask_and_max(s):
                if not s.has(-2):
                    dve.wait_ge(mask_added, 1)
                    dve.wait_ge(const_copied, 1)
                dve.wait_ge(scores_ready, s.at(1))
                nc.vector.scalar_tensor_tensor(
                    score[:, :, :], s_bank[:, 0:TOKENS].rearrange("p (j q) -> p q j", q=Q),
                    row_const[:, bass.ds(s.at(1, -1), 1)],
                    mask_add[:, bass.ds(s.at(TOKENS, -TOKENS), TOKENS)].rearrange("p (q j) -> p q j", q=Q),
                    ALU.add, ALU.add).then_inc(scores_read, 1)
                dve.wait_ge(scores_read, s.at(1))
                nc.vector.reduce_max(neg_top[:, :], score[:, :, :], AX.XY, negate=True).then_inc(top_ready, 1)
                dve.wait_ge(top_ready, s.at(1))
                nc.vector.tensor_scalar(neg_max[:, :], neg_top[:, :], -LEAST_MAX, None,
                                        ALU.min).then_inc(max_ready, 1)

            def normalise(s):
                dve.wait_ge(prob_ready, s.at(1))
                nc.vector.reciprocal(inv_total[:, :], total[:, :]).then_inc(inv_ready, 1)
                dve.wait_ge(inv_ready, s.at(1))
                if s.has(-2):
                    dve.wait_ge(w_col_loaded, s.at(16 * QUADS, -16 * QUADS))
                nc.vector.tensor_scalar(weight[:, :], prob[:, :], inv_total[:, :], None,
                                        ALU.mult).then_inc(weight_ready, 1)

            def spread(s):
                dve.wait_ge(w_col_loaded, s.at(16 * QUADS))
                nc.vector.tensor_tensor(
                    w_diag[:, s.slot(-1, 2), :, :], w_col[:, :].unsqueeze(2).to_broadcast([P, J, GROUP]),
                    row_mask[:, :].unsqueeze(1).to_broadcast([P, J, GROUP]),
                    ALU.mult).then_inc(w_diag_ready, 1)

            def step(s):
                for m in range(PAIRS):
                    if s.has(0):
                        if s.has(1) and m - 1 in DVE_CHUNKS:
                            copy_x(s, m - 1)
                        dve.wait_ge(relu_ready, s.at(PAIRS, m + 1))
                        nc.vector.scalar_tensor_tensor(
                            act_out[:, 2 * m:2 * m + 2, :].rearrange("p n t -> p (n t)"),
                            relu_neg[:, m % H_BANKS].rearrange("p n t -> p (n t)"), one_less_a[:, :],
                            h_bank[m % H_BANKS][:, 0:2 * TOKENS], ALU.mult, ALU.add).then_inc(act_ready, 1)
                        if s.has(1) and POOL_ROWS + m < GROUP:
                            build_w(s, POOL_ROWS + m)
                    if s.has(-1):
                        if m == PAIRS // 2 - 1:
                            mask_and_max(s)
                        if m == PAIRS // 2:
                            normalise(s)
                        if m == PAIRS - 1:
                            spread(s)

            nc.vector.memset(w2_slide[:, :], 0.0).then_inc(zeros_set, 1)
            nc.vector.memset(mask_b[:, :].bitcast(u16), 0x0101).then_inc(mask_cleared, 1)
            nc.vector.memset(s_bank[:, :], 0.0)
            nc.vector.memset(o_bank[:, :], 0.0).then_inc(zeros_set, 1)
            dve.wait_ge(ident_set, 2)
            nc.vector.reduce_sum(row_mask[:, :], ident[:, :].rearrange("p (b q) -> p b q", q=Q), AX.X)
            nc.vector.reduce_sum(quad_sum[:, :],
                                 ident[:, :].rearrange("p (g b) -> p b g", g=QUADS)[:, 0:GROUP], AX.X
                                 ).then_inc(masks_set, 1)
            dve.wait_ge(cand_turned, 1)
            for r in range(RUNS):
                copied = nc.vector.tensor_copy(
                    cand_bias[:, :, 0, QUADS * r:QUADS * (r + 1)],
                    h_bank[0][:, :].rearrange("d (k g r) -> d k g r", g=QUADS, r=RUNS)[:, :, :, r])
            copied.then_inc(cand_copied, 1)
            dve.wait_ge(small_loaded, 16 * 4)
            dve.wait_ge(bias_ready, 1)
            nc.vector.tensor_scalar(cand_bias[:, :, 1, :],
                                    h_bank[1][:, :].rearrange("h (k n) -> h k n", n=GROUP),
                                    b1[:, :], -1.0, ALU.add, ALU.mult).then_inc(bias_copied, 1)
            nc.vector.tensor_scalar(one_less_a[:, :], a[:, :], -1.0, 1.0,
                                    ALU.mult, ALU.add).then_inc(scalars_set, 1)
            first = Step(0, -1)
            for n in range(POOL_ROWS, GROUP):
                build_w(first, n)
            for c in DVE_CHUNKS:
                copy_x(first, c)
            dve.wait_ge(scalars_set, 1)
            dve.wait_ge(const_ready, 1)
            nc.vector.tensor_scalar(row_const[:, :], s_bank[:, 0:GROUPS], -1.0, b2[:, :],
                                    ALU.mult, ALU.add).then_inc(const_copied, 1)
            run_steps(dve, step)

        @block.tensor
        def _(pe):
            def turn_chunk(s, c):
                if c < T_BANKS:
                    if s.has(0):
                        pe.wait_ge(*chunk_copied(s.at, c + len(CHUNKS) - T_BANKS))
                else:
                    pe.wait_ge(*chunk_copied(lambda m, add: s.at(m, m + add), c - T_BANKS))
                if c == 0:
                    pe.wait_ge(x_loaded[s.slot(1)][0], s.lap_of(1, 16, 16))
                if CHUNKS[c][0] == X_CUT:
                    pe.wait_ge(x_loaded[s.slot(1)][1], s.lap_of(1, 16, 16))
                for i, j in enumerate(CHUNKS[c]):
                    done = nc.tensor.transpose(t_slot(s, c)[:, i * P:(i + 1) * P],
                                               x[:, s.slot(1), j * D:(j + 1) * D], ident[:, :])
                done.then_inc(turned, 1)

            def main(s, half):
                for n in range(half * HALF, (half + 1) * HALF):
                    m = n // 2
                    if s.has(0):
                        if n == 0:
                            pe.wait_ge(pool_w, s.at(1, 1))
                            pe.wait_ge(act_copied, s.at(len(ACT_CHUNKS), len(ACT_CHUNKS)))
                            pe.wait_ge(dve_copied, s.at(len(DVE_CHUNKS), len(DVE_CHUNKS)))
                        if n == POOL_ROWS:
                            pe.wait_ge(dve_w, s.at(1, 1))
                        if n % 2 == 0 and (s.has(-1) or m >= H_BANKS):
                            pe.wait_ge(act_ready, s.at(PAIRS, m + 1 - H_BANKS))
                        row = row_of(n)
                        done = nc.tensor.matmul(
                            h_bank[m % H_BANKS][:, (n % 2) * TOKENS:(n % 2 + 1) * TOKENS],
                            w_eff[:, s.slot(0, 2), n, :], xT[:, s.slot(0, 2), :, Q * row:Q * (row + 1)],
                            start=True, stop=True)
                        if n % 2 == 1:
                            done.then_inc(h_ready, 1)
                    if s.has(1) and n % 2 == 1 and m >= 1:
                        turn_chunk(s, m - 1)

            def dots(s, d, half):
                pe.wait_ge(act_ready, s.at(PAIRS, PAIRS * d + (half + 1) * PAIRS // 2))
                if half == 0 and s.has(d - 1):
                    pe.wait_ge(scores_read, s.at(1, d))
                for n in range(half * HALF, (half + 1) * HALF):
                    g, r = n % QUADS, n // QUADS
                    done = nc.tensor.matmul(s_bank[32 * g:32 * g + RUNS, 0:TOKENS],
                                            w2_slide[:, RUNS - 1 - r:2 * RUNS - 1 - r], act_out[:, n, :],
                                            start=(r == 0), stop=(r == RUNS - 1))
                if half == 1:
                    done.then_inc(scores_ready, 1)

            def weighted_sum(s):
                pe.wait_ge(w_diag_ready, s.at(1, -1))
                if s.has(-3):
                    pe.wait_ge(y_copied, s.at(1, -2))
                for j in range(J):
                    g = j % QUADS
                    done = nc.tensor.matmul(part_ps[32 * g:32 * g + GROUP, :], w_diag[:, s.slot(-2, 2), j, :],
                                            x[:, s.slot(-2), j * D:(j + 1) * D],
                                            start=(j < QUADS), stop=(j >= J - QUADS))
                done.then_inc(sum_ready, 1)

            def step(s):
                main(s, 0)
                if s.has(-1):
                    dots(s, -1, 1)
                if s.has(-2):
                    weighted_sum(s)
                main(s, 1)
                if s.has(0):
                    dots(s, 0, 0)
                if s.has(-2):
                    pe.wait_ge(part_copied, s.at(1, -1))
                    nc.tensor.matmul(y_ps, quad_sum[:, :], part[:, :], start=True,
                                     stop=True).then_inc(y_ready, 1)

            pe.wait_ge(ident_set, 2)
            pe.wait_ge(cand_loaded, 16)
            for c in range(ROWS // P):
                done = nc.tensor.transpose(h_bank[0][:, c * P:(c + 1) * P], cand[:, c, :], ident[:, :])
            done.then_inc(cand_turned, 1)
            pe.wait_ge(w1_loaded, 16)
            pe.wait_ge(cand_copied, 1)
            nc.tensor.matmul(h_bank[1][:, :], w1[:, 1, :], cand_bias[:, :, 0, :], start=True,
                             stop=True).then_inc(bias_ready, 1)
            for c in range(len(CHUNKS)):
                turn_chunk(Step(0, -1), c)
            pe.wait_ge(small_loaded, 16 * 4)
            pe.wait_ge(zeros_set, 2)
            pe.wait_ge(bias_copied, 1)
            for n in range(GROUP):
                g, r = n % QUADS, n // QUADS
                done = nc.tensor.matmul(s_bank[32 * g:32 * g + RUNS, 0:GROUPS],
                                        w2_slide[:, RUNS - 1 - r:2 * RUNS - 1 - r], cand_bias[:, :, 1, n],
                                        start=(r == 0), stop=(r == RUNS - 1))
            done.then_inc(const_ready, 1)
            pe.wait_ge(const_copied, 1)
            pe.wait_ge(masks_set, 1)
            run_steps(pe, step)


def kernel(**inputs):
    import numpy as np
    import concourse.bacc as bacc
    from concourse.bass_utils import run_bass_kernel_spmd

    names = ["r_transformer_out", "r_candidate", "r_mask", "L0_rec_W1", "L0_rec_b1", "L0_rec_a",
             "L0_rec_W2", "L0_rec_b2"]
    nc = bacc.Bacc("TRN2", target_bir_lowering=False, num_devices=1)
    arrays, args = {}, []
    for name in names:
        array = np.ascontiguousarray(inputs[name])
        array = array.reshape(array.shape or (1,))
        arrays[name] = array
        args.append(nc.dram_tensor(name, array.shape, mybir.dt.from_np(array.dtype), kind="ExternalInput").ap())
    args.append(nc.dram_tensor("out", (ROWS, D), mybir.dt.float32, kind="ExternalOutput").ap())
    build(nc, *args)
    result = run_bass_kernel_spmd(nc, [arrays], core_ids=[0])
    return result.results[0]["out"]
```

```python
from contextlib import ExitStack

import concourse.bass as bass
from concourse import mybir

ROWS, TOKENS, D, H = 512, 200, 128, 128
P = 128
GROUP = 16
GROUPS = ROWS // GROUP
Q = P // GROUP
J = TOKENS // Q
QUADS = 4
RUNS = GROUP // QUADS
PAIRS = GROUP // 2
HALF = GROUP // 2

X_SLOTS = 4
X_CUT = 12
H_BANKS = 4
T_BANKS = 2
T_BATCH = 4
CHUNK_PAIR = [1, 2, 3, 4, 5, 6, 6]
CHUNKS = [list(range(j, min(j + T_BATCH, J))) for j in range(0, J, T_BATCH)]
ACT_AFTER = {0: 1, 2: 3, 3: 4, 5: 6}
DVE_BEFORE = {1: 2, 4: 5, 6: 7}
ACT_CHUNKS, DVE_CHUNKS = list(ACT_AFTER), list(DVE_BEFORE)
POOL_ROWS = 10
POOL_FIRST = 4
LAPS = (2, 30)
MASK_AFTER = [[3, 5, 7], [1, 3, 5, 6, 7]]
MASK_CUTS = sum(map(len, MASK_AFTER))
MASK_CUT = GROUPS // MASK_CUTS
MASKED = -3e38
LEAST_MAX = -1e38


def row_of(n):
    return RUNS * (n % QUADS) + n // QUADS


class Step:

    def __init__(self, lap, c):
        self.lap, self.c = lap, c

    def at(self, mult, add=0):
        return self.lap * (X_SLOTS * mult) + (self.c * mult + add)

    def lap_of(self, d, mult, add=0):
        return self.lap * mult + ((self.c + d) // X_SLOTS * mult + add)

    def slot(self, d, n=X_SLOTS):
        return (self.c + d) % n

    def ends_four(self):
        return self.has(-2) and self.slot(-2) == QUADS - 1

    def has(self, d):
        return not isinstance(self.lap, int) or 0 <= self.c + d < GROUPS


def run_steps(engine, step):
    for c in range(0, LAPS[0]):
        step(Step(0, c))
    with engine.Fori(0, (LAPS[1] - LAPS[0]) // X_SLOTS) as lap:
        for c in range(LAPS[0], LAPS[0] + X_SLOTS):
            step(Step(lap, c))
    for c in range(LAPS[1], GROUPS + 2):
        step(Step(0, c))


def build(nc, x_in, cand_in, mask_in, w1_in, b1_in, a_in, w2_in, b2_in, out):
    f32, bf16, u8, u16 = mybir.dt.float32, mybir.dt.bfloat16, mybir.dt.uint8, mybir.dt.uint16
    ALU, ACT, AX = mybir.AluOpType, mybir.ActivationFunctionType, mybir.AxisListType

    x_groups = x_in.rearrange("b t d -> (b t) d").rearrange("(k p j) d -> k p (j d)", p=P, j=J)
    out_groups = out.rearrange("(k b) d -> k b d", b=GROUP)
    mask_quads = mask_in.rearrange("(k g r) t -> g r k t", g=QUADS, r=RUNS)

    with ExitStack() as ctx:
        def sb(name, shape, dt=f32):
            return ctx.enter_context(nc.sbuf_tensor(name, shape, dt))

        def sem(name):
            return ctx.enter_context(nc.semaphore(name))

        x = sb("x", [P, X_SLOTS, J * D])
        xT = sb("xT", [P, 2, J, P])
        w_eff = sb("w_eff", [P, 2, GROUP, H])
        relu_neg = sb("relu_neg", [P, H_BANKS, 2, TOKENS])
        act_out = sb("act_out", [P, GROUP, TOKENS])
        cand_bias = sb("cand_bias", [P, GROUPS, 2, GROUP])
        stage = sb("stage", [P, X_SLOTS, 2, GROUP])
        mask_b = sb("mask_b", [P, GROUPS * TOKENS], u8)
        mask_add = sb("mask_add", [P, GROUPS * TOKENS], bf16)
        score = sb("score", [P, Q, J])
        prob = sb("prob", [P, TOKENS])
        weight = sb("weight", [P, TOKENS])
        w_col = sb("w_col", [P, J])
        w_diag = sb("w_diag", [P, 2, J, GROUP])
        part = sb("part", [P, X_SLOTS, D])
        y = sb("y", [P, D])
        cand = sb("cand", [P, ROWS // P, D])
        w1 = sb("w1", [P, 3, H])
        w2_slide = sb("w2_slide", [P, 2 * RUNS - 1])
        ident = sb("ident", [P, P])
        row_mask = sb("row_mask", [P, GROUP])
        quad_sum = sb("quad_sum", [P, GROUP])
        b1 = sb("b1", [P, 1])
        a = sb("a", [P, 1])
        one_less_a = sb("one_less_a", [P, 1])
        b2 = sb("b2", [P, 1])
        row_const = sb("row_const", [P, GROUPS])
        neg_top = sb("neg_top", [P, 1])
        neg_max = sb("neg_max", [P, 1])
        total = sb("total", [P, 1])
        inv_total = sb("inv_total", [P, 1])

        t_bank = [ctx.enter_context(nc.psum_tensor(f"t_bank{i}", [P, 512], f32)) for i in range(T_BANKS)]
        h_bank = [ctx.enter_context(nc.psum_tensor(f"h_bank{i}", [P, 512], f32)) for i in range(H_BANKS)]
        s_bank = ctx.enter_context(nc.psum_tensor("s_bank", [P, 512], f32))
        o_bank = ctx.enter_context(nc.psum_tensor("o_bank", [P, 512], f32))
        part_ps, y_ps = o_bank[:, 0:D], o_bank[:, D:2 * D]

        x_loaded = [[sem(f"x_loaded{s}_{h}") for h in range(2)] for s in range(X_SLOTS)]
        cand_loaded, w1_loaded, b1_loaded, w2_loaded = (
            sem("cand_loaded"), sem("w1_loaded"), sem("b1_loaded"), sem("w2_loaded"))
        scalars_loaded, mask_loaded = sem("scalars_loaded"), sem("mask_loaded")
        zeros_set, ident_set, masks_set = sem("zeros_set"), sem("ident_set"), sem("masks_set")
        mask_cleared, mask_added = sem("mask_cleared"), sem("mask_added")
        cand_turned, cand_copied = sem("cand_turned"), sem("cand_copied")
        bias_ready, bias_copied = sem("bias_ready"), sem("bias_copied")
        const_ready, const_copied, scalars_set = sem("const_ready"), sem("const_copied"), sem("scalars_set")
        staged = sem("staged")
        pool_mult = sem("pool_mult")
        pool_w, dve_w = sem("pool_w"), sem("dve_w")
        turned = sem("turned")
        act_copied, dve_copied = sem("act_copied"), sem("dve_copied")
        h_ready = sem("h_ready")
        relu_ready = sem("relu_ready")
        act_ready = sem("act_ready")
        scores_ready = sem("scores_ready")
        scores_read = sem("scores_read")
        top_ready = sem("top_ready")
        max_ready, prob_ready, inv_ready, weight_ready = (
            sem("max_ready"), sem("prob_ready"), sem("inv_ready"), sem("weight_ready"))
        w_col_loaded, w_diag_ready = sem("w_col_loaded"), sem("w_diag_ready")
        sum_ready = sem("sum_ready")
        part_copied, y_ready, y_copied = sem("part_copied"), sem("y_ready"), sem("y_copied")
        stored = sem("stored")

        def chunk_copied(L_at, c):
            if c in ACT_CHUNKS:
                return act_copied, L_at(len(ACT_CHUNKS), ACT_CHUNKS.index(c) + 1)
            return dve_copied, L_at(len(DVE_CHUNKS), DVE_CHUNKS.index(c) + 1)

        def t_slot(s, c):
            return t_bank[(s.slot(1, 2) + c) % T_BANKS]

        def copy_chunk(copy, s, c):
            j, n = CHUNKS[c][0], len(CHUNKS[c])
            return copy(xT[:, s.slot(1, 2), j:j + n, :],
                        t_slot(s, c)[:, 0:n * P].rearrange("d (j p) -> d j p", p=P))

        block = ctx.enter_context(nc.Block())

        @block.sync
        def _(sp):
            def load_x(s, d):
                slot = s.slot(d)
                src = x_groups[bass.ds(s.at(1, d), 1)].rearrange("k p n -> (k p) n")
                for h, (lo, hi) in enumerate(((0, X_CUT * D), (X_CUT * D, J * D))):
                    sp.dma_start(x[:, slot, lo:hi], src[:, lo:hi]).then_inc(x_loaded[slot][h], 16)

            sp.dma_start(cand[:, :, :], cand_in.rearrange("(c p) d -> p c d", p=P)).then_inc(cand_loaded, 16)
            sp.dma_start(w1[:, :, :], w1_in.rearrange("(s d) h -> d s h", d=D)).then_inc(w1_loaded, 16)
            load_x(Step(0, 0), 0)
            load_x(Step(0, 0), 1)
            sp.wait_ge(mask_cleared, 1)
            for g in range(QUADS):
                sp.dma_start(mask_b[32 * g:32 * g + RUNS, :].rearrange("r (k t) -> r k t", t=TOKENS),
                             mask_quads[g]).then_inc(mask_loaded, 16)

            def step(s):
                if s.has(2):
                    if s.has(-2):
                        sp.wait_ge(sum_ready, s.at(1, -1))
                    load_x(s, 2)
                if s.has(-1):
                    sp.wait_ge(weight_ready, s.at(1))
                    for g in range(QUADS):
                        sp.dma_start(w_col[32 * g:32 * g + 32, :],
                                     weight[32 * g:32 * g + RUNS, :]).then_inc(w_col_loaded, 16)
                if s.ends_four():
                    sp.wait_ge(y_copied, s.lap_of(-2, 1, 1))
                    for u in range(QUADS):
                        sp.dma_start(out_groups[bass.ds(s.at(1, u - 5), 1)].rearrange("k b d -> (k b) d"),
                                     y[32 * u:32 * u + GROUP, :]).then_inc(stored, 16)

            run_steps(sp, step)
            sp.wait_ge(stored, 16 * GROUPS)

        @block.gpsimd
        def _(pool):
            nc.gpsimd.memset(ident[:, :], 0.0).then_inc(ident_set, 1)
            pool.wait_ge(ident_set, 1)
            nc.gpsimd.affine_select(out=ident[:, :], in_=ident[:, :], compare_op=ALU.not_equal, fill=1.0,
                                    base=0, pattern=[[-1, P]], channel_multiplier=1).then_inc(ident_set, 1)
            nc.gpsimd.memset(mask_b[:, :].bitcast(u16), 0x0101).then_inc(mask_cleared, 1)

            def step(s):
                if not s.has(1):
                    return
                if s.has(-1):
                    pool.wait_ge(h_ready, s.at(PAIRS))
                src = cand_bias[:, bass.ds(s.at(1, 1), 1)].rearrange("p k s n -> p (k s n)")
                nc.gpsimd.tensor_copy(stage[:, s.slot(1)].rearrange("p s n -> p (s n)"),
                                      src).then_inc(staged, 1)
                if s.has(0):
                    pool.wait_ge(staged, s.at(1, 2))
                    build_w(s, POOL_ROWS, stage[:, s.slot(1), 0, 0:POOL_ROWS])

            def build_w(s, n, cands):
                rows = w_eff[:, s.slot(1, 2), 0:n, :]
                nc.gpsimd.tensor_tensor(rows, w1[:, 2:3, :].to_broadcast([P, n, H]),
                                        cands.unsqueeze(2).to_broadcast([P, n, H]),
                                        ALU.mult).then_inc(pool_mult, 1)
                pool.wait_ge(pool_mult, s.at(1, 2))
                nc.gpsimd.tensor_tensor(rows, rows, w1[:, 0:1, :].to_broadcast([P, n, H]),
                                        ALU.add).then_inc(pool_w, 1)

            pool.wait_ge(w1_loaded, 16)
            pool.wait_ge(cand_copied, 1)
            build_w(Step(0, -1), POOL_FIRST, cand_bias[:, 0, 0, 0:POOL_FIRST])
            pool.wait_ge(bias_copied, 1)
            step(Step(0, -1))
            run_steps(pool, step)

        @block.scalar
        def _(act):
            act.dma_start(b1[:, :], b1_in.rearrange("(h o) -> h o", o=1)).then_inc(b1_loaded, 16)
            act.wait_ge(zeros_set, 1)
            act.dma_start(w2_slide[:, RUNS - 1:RUNS], w2_in).then_inc(w2_loaded, 16)
            act.dma_start(a[:, :], a_in.partition_broadcast(P)).then_inc(scalars_loaded, 16)
            act.dma_start(b2[:, :], b2_in.partition_broadcast(P)).then_inc(scalars_loaded, 16)

            def copy_x(s, c):
                act.wait_ge(turned, s.at(len(CHUNKS), len(CHUNKS) + c + 1))
                if c == ACT_CHUNKS[0] and s.has(-1):
                    act.wait_ge(h_ready, s.at(PAIRS))
                copy_chunk(nc.scalar.copy, s, c).then_inc(act_copied, 1)

            def add_mask(i):
                if i == 0:
                    act.wait_ge(mask_loaded, 16 * QUADS)
                cut = slice(i * MASK_CUT * TOKENS, (i + 1) * MASK_CUT * TOKENS)
                nc.scalar.activation(mask_add[:, cut], mask_b[:, cut], ACT.Copy,
                                     scale=-MASKED, bias=MASKED).then_inc(mask_added, 1)

            def step(s):
                for m in range(PAIRS):
                    if s.has(0):
                        if m == 0:
                            act.wait_ge(staged, s.at(1, 1))
                        act.wait_ge(h_ready, s.at(PAIRS, m + 1))
                        for n in (2 * m, 2 * m + 1):
                            relu = nc.scalar.activation(
                                relu_neg[:, m % H_BANKS, n % 2, :],
                                h_bank[m % H_BANKS][:, (n % 2) * TOKENS:(n % 2 + 1) * TOKENS], ACT.Relu,
                                scale=-1.0, bias=stage[:, s.slot(0), 1, n:n + 1])
                        relu.then_inc(relu_ready, 1)
                        for c in ACT_CHUNKS:
                            if s.has(1) and m == ACT_AFTER[c]:
                                copy_x(s, c)
                    if not s.has(-2) and m in MASK_AFTER[s.c]:
                        add_mask(s.c * len(MASK_AFTER[0]) + MASK_AFTER[s.c].index(m))
                    if m == PAIRS // 2 - 1 and s.has(-1):
                        act.wait_ge(max_ready, s.at(1))
                        nc.scalar.activation(prob[:, :], score[:, :, :].rearrange("p q j -> p (q j)"),
                                             ACT.Exp, bias=neg_max[:, :], accum_out=total[:, :]
                                             ).then_inc(prob_ready, 1)
                    if m == PAIRS // 2 - 1 and s.has(-2):
                        act.wait_ge(sum_ready, s.at(1, -1))
                        nc.scalar.copy(part[:, s.slot(-2), :], part_ps).then_inc(part_copied, 1)
                if s.ends_four():
                    act.wait_ge(y_ready, s.lap_of(-2, 1, 1))
                    if s.has(-6):
                        act.wait_ge(stored, s.lap_of(-2, 16 * QUADS))
                    nc.scalar.copy(y[:, :], y_ps).then_inc(y_copied, 1)

            for c in ACT_CHUNKS:
                copy_x(Step(0, -1), c)
            run_steps(act, step)

        @block.vector
        def _(dve):
            def copy_x(s, c):
                dve.wait_ge(turned, s.at(len(CHUNKS), len(CHUNKS) + c + 1))
                if c == DVE_CHUNKS[0] and s.has(-1):
                    dve.wait_ge(h_ready, s.at(PAIRS))
                copy_chunk(nc.vector.tensor_copy, s, c).then_inc(dve_copied, 1)

            def build_w(s, n):
                if s.has(0) and n == POOL_ROWS:
                    dve.wait_ge(staged, s.at(1, 2))
                    if s.has(-1):
                        dve.wait_ge(h_ready, s.at(PAIRS))
                c = stage[:, s.slot(1), 0, n:n + 1] if s.has(0) else cand_bias[:, 0, 0, n:n + 1]
                made = nc.vector.scalar_tensor_tensor(
                    w_eff[:, s.slot(1, 2), n, :], w1[:, 2, :], c, w1[:, 0, :], ALU.mult, ALU.add)
                if n == GROUP - 1:
                    made.then_inc(dve_w, 1)

            def mask_and_max(s):
                if not s.has(-2):
                    dve.wait_ge(mask_added, len(MASK_AFTER[0]))
                    dve.wait_ge(masks_set, 1)
                    dve.wait_ge(const_copied, 1)
                dve.wait_ge(scores_ready, s.at(1))
                nc.vector.scalar_tensor_tensor(
                    score[:, :, :], s_bank[:, 0:TOKENS].rearrange("p (j q) -> p q j", q=Q),
                    row_const[:, bass.ds(s.at(1, -1), 1)],
                    mask_add[:, bass.ds(s.at(TOKENS, -TOKENS), TOKENS)].rearrange("p (q j) -> p q j", q=Q),
                    ALU.add, ALU.add).then_inc(scores_read, 1)
                dve.wait_ge(scores_read, s.at(1))
                nc.vector.reduce_max(neg_top[:, :], score[:, :, :], AX.XY, negate=True).then_inc(top_ready, 1)
                dve.wait_ge(top_ready, s.at(1))
                nc.vector.tensor_scalar(neg_max[:, :], neg_top[:, :], -LEAST_MAX, None,
                                        ALU.min).then_inc(max_ready, 1)

            def normalise(s):
                dve.wait_ge(prob_ready, s.at(1))
                nc.vector.reciprocal(inv_total[:, :], total[:, :]).then_inc(inv_ready, 1)
                dve.wait_ge(inv_ready, s.at(1))
                if s.has(-2):
                    dve.wait_ge(w_col_loaded, s.at(16 * QUADS, -16 * QUADS))
                nc.vector.tensor_scalar(weight[:, :], prob[:, :], inv_total[:, :], None,
                                        ALU.mult).then_inc(weight_ready, 1)

            def spread(s):
                dve.wait_ge(w_col_loaded, s.at(16 * QUADS))
                nc.vector.tensor_tensor(
                    w_diag[:, s.slot(-1, 2), :, :], w_col[:, :].unsqueeze(2).to_broadcast([P, J, GROUP]),
                    row_mask[:, :].unsqueeze(1).to_broadcast([P, J, GROUP]),
                    ALU.mult).then_inc(w_diag_ready, 1)

            def step(s):
                for m in range(PAIRS):
                    if m == PAIRS // 2 and s.has(-1):
                        normalise(s)
                    if s.has(0):
                        for c in DVE_CHUNKS:
                            if s.has(1) and m == DVE_BEFORE[c]:
                                copy_x(s, c)
                        dve.wait_ge(relu_ready, s.at(PAIRS, m + 1))
                        nc.vector.scalar_tensor_tensor(
                            act_out[:, 2 * m:2 * m + 2, :].rearrange("p n t -> p (n t)"),
                            relu_neg[:, m % H_BANKS].rearrange("p n t -> p (n t)"), one_less_a[:, :],
                            h_bank[m % H_BANKS][:, 0:2 * TOKENS], ALU.mult, ALU.add).then_inc(act_ready, 1)
                        if s.has(1) and POOL_ROWS + m < GROUP:
                            build_w(s, POOL_ROWS + m)
                    if s.has(-1):
                        if m == PAIRS // 2 - 1:
                            mask_and_max(s)
                        if m == PAIRS - 1:
                            spread(s)
                            if not s.has(-2):
                                dve.wait_ge(mask_added, MASK_CUTS)

            nc.vector.memset(w2_slide[:, :], 0.0).then_inc(zeros_set, 1)
            nc.vector.memset(s_bank[:, 0:TOKENS], 0.0)
            nc.vector.memset(o_bank[:, 0:2 * D], 0.0).then_inc(zeros_set, 1)
            dve.wait_ge(ident_set, 2)
            nc.vector.reduce_sum(row_mask[:, :], ident[:, :].rearrange("p (b q) -> p b q", q=Q), AX.X)
            nc.vector.reduce_sum(quad_sum[:, :],
                                 ident[:, :].rearrange("p (g b) -> p b g", g=QUADS)[:, 0:GROUP], AX.X
                                 ).then_inc(masks_set, 1)
            dve.wait_ge(cand_turned, 1)
            for r in range(RUNS):
                copied = nc.vector.tensor_copy(
                    cand_bias[:, :, 0, QUADS * r:QUADS * (r + 1)],
                    h_bank[0][:, :].rearrange("d (k g r) -> d k g r", g=QUADS, r=RUNS)[:, :, :, r])
            copied.then_inc(cand_copied, 1)
            dve.wait_ge(cand_copied, 1)
            dve.wait_ge(w1_loaded, 16)
            first = Step(0, -1)
            for n in range(POOL_FIRST, GROUP // 2):
                build_w(first, n)
            dve.wait_ge(b1_loaded, 16)
            dve.wait_ge(bias_ready, 1)
            nc.vector.tensor_scalar(cand_bias[:, :, 1, :],
                                    h_bank[1][:, :].rearrange("h (k n) -> h k n", n=GROUP),
                                    b1[:, :], -1.0, ALU.add, ALU.mult).then_inc(bias_copied, 1)
            for c, rows in zip(DVE_CHUNKS, ((8, 11), (11, 14), (14, 16))):
                for n in range(*rows):
                    build_w(first, n)
                copy_x(first, c)
            dve.wait_ge(scalars_loaded, 32)
            nc.vector.tensor_scalar(one_less_a[:, :], a[:, :], -1.0, 1.0,
                                    ALU.mult, ALU.add).then_inc(scalars_set, 1)
            dve.wait_ge(scalars_set, 1)
            dve.wait_ge(const_ready, 1)
            nc.vector.tensor_scalar(row_const[:, :], s_bank[:, 0:GROUPS], -1.0, b2[:, :],
                                    ALU.mult, ALU.add).then_inc(const_copied, 1)
            run_steps(dve, step)

        @block.tensor
        def _(pe):
            def turn_chunk(s, c):
                if c < T_BANKS:
                    if s.has(0):
                        pe.wait_ge(*chunk_copied(s.at, c + len(CHUNKS) - T_BANKS))
                else:
                    pe.wait_ge(*chunk_copied(lambda m, add: s.at(m, m + add), c - T_BANKS))
                if c == 0:
                    pe.wait_ge(x_loaded[s.slot(1)][0], s.lap_of(1, 16, 16))
                if CHUNKS[c][0] == X_CUT:
                    pe.wait_ge(x_loaded[s.slot(1)][1], s.lap_of(1, 16, 16))
                for i, j in enumerate(CHUNKS[c]):
                    done = nc.tensor.transpose(t_slot(s, c)[:, i * P:(i + 1) * P],
                                               x[:, s.slot(1), j * D:(j + 1) * D], ident[:, :])
                done.then_inc(turned, 1)

            def main(s, half):
                for n in range(half * HALF, (half + 1) * HALF):
                    m = n // 2
                    if s.has(0):
                        if n == 0:
                            pe.wait_ge(pool_w, s.at(1, 1))
                            pe.wait_ge(act_copied, s.at(len(ACT_CHUNKS), len(ACT_CHUNKS)))
                            pe.wait_ge(dve_copied, s.at(len(DVE_CHUNKS), len(DVE_CHUNKS)))
                        if n == POOL_ROWS:
                            pe.wait_ge(dve_w, s.at(1, 1))
                        if n % 2 == 0 and (s.has(-1) or m >= H_BANKS):
                            pe.wait_ge(act_ready, s.at(PAIRS, m + 1 - H_BANKS))
                        row = row_of(n)
                        done = nc.tensor.matmul(
                            h_bank[m % H_BANKS][:, (n % 2) * TOKENS:(n % 2 + 1) * TOKENS],
                            w_eff[:, s.slot(0, 2), n, :], xT[:, s.slot(0, 2), :, Q * row:Q * (row + 1)],
                            start=True, stop=True)
                        if n % 2 == 1:
                            done.then_inc(h_ready, 1)
                    for c in range(len(CHUNKS)):
                        if s.has(1) and n % 2 == 1 and m == CHUNK_PAIR[c]:
                            turn_chunk(s, c)

            def dots(s, d, half):
                pe.wait_ge(act_ready, s.at(PAIRS, PAIRS * d + (half + 1) * PAIRS // 2))
                if half == 0 and s.has(d - 1):
                    pe.wait_ge(scores_read, s.at(1, d))
                elif half == 0:
                    pe.wait_ge(const_copied, 1)
                    pe.wait_ge(masks_set, 1)
                for n in range(half * HALF, (half + 1) * HALF):
                    g, r = n % QUADS, n // QUADS
                    done = nc.tensor.matmul(s_bank[32 * g:32 * g + RUNS, 0:TOKENS],
                                            w2_slide[:, RUNS - 1 - r:2 * RUNS - 1 - r], act_out[:, n, :],
                                            start=(r == 0), stop=(r == RUNS - 1))
                if half == 1:
                    done.then_inc(scores_ready, 1)

            def weighted_sum(s):
                pe.wait_ge(w_diag_ready, s.at(1, -1))
                if s.has(-3):
                    pe.wait_ge(part_copied, s.at(1, -2))
                    if s.slot(-2) == 0:
                        pe.wait_ge(y_copied, s.lap_of(-2, 1))
                for j in range(J):
                    g = j % QUADS
                    done = nc.tensor.matmul(part_ps[32 * g:32 * g + GROUP, :], w_diag[:, s.slot(-2, 2), j, :],
                                            x[:, s.slot(-2), j * D:(j + 1) * D],
                                            start=(j < QUADS), stop=(j >= J - QUADS))
                done.then_inc(sum_ready, 1)

            def step(s):
                main(s, 0)
                if s.has(-1):
                    dots(s, -1, 1)
                if s.has(-2):
                    weighted_sum(s)
                main(s, 1)
                if s.has(0):
                    dots(s, 0, 0)
                if s.ends_four():
                    pe.wait_ge(part_copied, s.at(1, -1))
                    for u in range(QUADS):
                        done = nc.tensor.matmul(y_ps[32 * u:32 * u + GROUP, :], quad_sum[:, :],
                                                part[:, u, :], start=True, stop=True)
                    done.then_inc(y_ready, 1)

            pe.wait_ge(ident_set, 2)
            pe.wait_ge(cand_loaded, 16)
            for c in range(ROWS // P):
                done = nc.tensor.transpose(h_bank[0][:, c * P:(c + 1) * P], cand[:, c, :], ident[:, :])
            done.then_inc(cand_turned, 1)
            pe.wait_ge(w1_loaded, 16)
            pe.wait_ge(cand_copied, 1)
            nc.tensor.matmul(h_bank[1][:, :], w1[:, 1, :], cand_bias[:, :, 0, :], start=True,
                             stop=True).then_inc(bias_ready, 1)
            for c in range(len(CHUNKS)):
                turn_chunk(Step(0, -1), c)
            pe.wait_ge(w2_loaded, 16)
            pe.wait_ge(zeros_set, 2)
            pe.wait_ge(bias_copied, 1)
            for n in range(GROUP):
                g, r = n % QUADS, n // QUADS
                done = nc.tensor.matmul(s_bank[32 * g:32 * g + RUNS, 0:GROUPS],
                                        w2_slide[:, RUNS - 1 - r:2 * RUNS - 1 - r], cand_bias[:, :, 1, n],
                                        start=(r == 0), stop=(r == RUNS - 1))
            done.then_inc(const_ready, 1)
            run_steps(pe, step)


def kernel(**inputs):
    import numpy as np
    import concourse.bacc as bacc
    from concourse.bass_utils import run_bass_kernel_spmd

    names = ["r_transformer_out", "r_candidate", "r_mask", "L0_rec_W1", "L0_rec_b1", "L0_rec_a",
             "L0_rec_W2", "L0_rec_b2"]
    nc = bacc.Bacc("TRN2", target_bir_lowering=False, num_devices=1)
    arrays, args = {}, []
    for name in names:
        array = np.ascontiguousarray(inputs[name])
        array = array.reshape(array.shape or (1,))
        arrays[name] = array
        args.append(nc.dram_tensor(name, array.shape, mybir.dt.from_np(array.dtype), kind="ExternalInput").ap())
    args.append(nc.dram_tensor("out", (ROWS, D), mybir.dt.float32, kind="ExternalOutput").ap())
    build(nc, *args)
    result = run_bass_kernel_spmd(nc, [arrays], core_ids=[0])
    return result.results[0]["out"]
```
